# Optimizing a Trainium2 kernel written in Bass

```python
import numpy as np
import jax
import jax.numpy as jnp

def _softmax(x, axis=-1):
    return jax.nn.softmax(x, axis=axis)

def _gelu(x):
    return jax.nn.gelu(x, approximate=True)

def _silu(x):
    return jax.nn.silu(x)

def _sigmoid(x):
    return jax.nn.sigmoid(x)

def _layernorm(x, axis=-1, eps=1e-05):
    m = jnp.mean(x, axis=axis, keepdims=True)
    v = jnp.var(x, axis=axis, keepdims=True)
    return (x - m) / jnp.sqrt(v + eps)

def _scatter_add(tgt, idx, src, axis=0):
    return tgt.at[idx].add(src)

def _segment_sum(src, seg, n):
    return jax.ops.segment_sum(src, seg, n)
kernel_name = 'mk_adj_preln_d1_adj_r2_c908dc'

def setup_inputs(seed: int=0):
    np.random.seed(seed)
    _w = jnp.asarray

    def _rec_inputs():
        import jax
        import jax.numpy as jnp
        _gk = jax.random.key(seed)
        x = -8.776e-05 + 1 * jax.random.normal(jax.random.fold_in(_gk, 1), (10000, 128), jnp.float32)
        _a = jax.random.bernoulli(jax.random.fold_in(_gk, 2), 0.0002, (10000, 10000))
        _a = jnp.logical_or(_a, jnp.eye(10000, dtype=bool))
        _af = _a.astype(jnp.float32)
        _af = _af * jax.random.uniform(jax.random.fold_in(_gk, 3), (10000, 10000), jnp.float32, 0.05, 1)
        adj = _af
        return (x, adj)
    x, adj = _rec_inputs()

    def _L0_gnn_setup():
        import jax, jax.numpy as jnp
        import numpy as np
        N_USER = 10000
        N_ITEM = 10000
        HID = 128
        key = jax.random.key(seed)
        k1, k2, k3, k4, k5, k6, k7 = jax.random.split(key, 7)
        scale = 1.0 / np.sqrt(HID)
        return {'user_feat': jax.random.normal(k1, (N_USER, HID), dtype=jnp.float32), 'item_feat': jax.random.normal(k2, (N_ITEM, HID), dtype=jnp.float32), 'adj': jax.random.uniform(k3, (N_USER, N_ITEM), dtype=jnp.float32), 'W_item': jax.random.uniform(k4, (HID, HID), dtype=jnp.float32, minval=-scale, maxval=scale), 'b_item': jax.random.uniform(k5, (HID,), dtype=jnp.float32, minval=-scale, maxval=scale), 'W_user': jax.random.uniform(k6, (HID, HID), dtype=jnp.float32, minval=-scale, maxval=scale), 'b_user': jax.random.uniform(k7, (HID,), dtype=jnp.float32, minval=-scale, maxval=scale)}
    _L0_gnn_all = _L0_gnn_setup()
    _L0_gnn_in = {k: v for k, v in _L0_gnn_all.items() if k in ('item_feat', 'W_item', 'b_item', 'W_user', 'b_user')}
    del _L0_gnn_all
    return {'x': x, 'adj': adj, 'L0_gnn_item_feat': _L0_gnn_in['item_feat'], 'L0_gnn_W_item': _L0_gnn_in['W_item'], 'L0_gnn_b_item': _L0_gnn_in['b_item'], 'L0_gnn_W_user': _L0_gnn_in['W_user'], 'L0_gnn_b_user': _L0_gnn_in['b_user']}

def reference(x, adj, L0_gnn_item_feat, L0_gnn_W_item, L0_gnn_b_item, L0_gnn_W_user, L0_gnn_b_user):
    import jax
    import jax.numpy as jnp

    def _L0_gnn_ref(user_feat, item_feat, adj, W_item, b_item, W_user, b_user):
        import jax, jax.numpy as jnp
        import numpy as np
        N_USER = 10000
        N_ITEM = 10000
        HID = 128
        h = item_feat @ W_item.T + b_item
        b = user_feat @ W_user.T + b_user
        return jax.nn.relu(adj @ h + b)
    h = jnp.maximum(_layernorm(x, axis=-1), 0.0)
    x = x + _L0_gnn_ref(h, L0_gnn_item_feat, adj, L0_gnn_W_item, L0_gnn_b_item, L0_gnn_W_user, L0_gnn_b_user)
    return x

_drawn_inputs = setup_inputs


def setup_inputs(seed=0):
    import zlib

    import numpy as np

    out = dict(_drawn_inputs(seed))
    spreads = {}
    factors = {}
    for name, (base, spread) in spreads.items():
        noise = np.random.default_rng([zlib.crc32(name.encode()), seed]).standard_normal(out[name].shape)
        drawn = base * np.exp(spread * noise) if base else spread * noise
        out[name] = jnp.asarray(drawn.astype(out[name].dtype))
    for name, factor in factors.items():
        out[name] = (out[name] * factor).astype(out[name].dtype)
    return out
```

```python
import concourse.bass as bass
from concourse import mybir
from contextlib import ExitStack

USERS, ITEMS, HID = 10000, 10000, 128
P = 128
BLOCKS = 20
UB = USERS // BLOCKS
XT = 4
UT = UB // XT
TILES = ITEMS // P
REST = ITEMS - TILES * P
CHUNKS = 20
CT = -(-TILES // CHUNKS)
SHORT = CHUNKS * CT - TILES
CHUNK_TILES = [CT] * (CHUNKS - SHORT) + [CT - 1] * SHORT
CHUNK_AT = [sum(CHUNK_TILES[:c]) for c in range(CHUNKS)]
HG = 6
GROUPS = TILES // HG
EPS = 1e-5

RAW_SLOTS, HI_SLOTS, LO_SLOTS, FEAT_SLOTS = 5, 4, 2, 3
RAW_USES = CHUNKS // RAW_SLOTS

RELU_AFTER, SUM_AFTER, STATS_AFTER, MOMENTS_AFTER, STD_AFTER, SCALE_AFTER, NORM_AFTER = 4, 5, 6, 7, 9, 10, 12
TRANSPOSE_BEFORE, EVACUATE_AFTER, EXTRA_BEFORE = 14, 16, 19
STORE_BEFORE = 9


def gnn_kernel(nc, adjt, adjt_rest, featt, xt, w_item_t, w_user_t, b_item, b_user, out):
    fp32, fp32r = mybir.dt.float32, mybir.dt.float32r
    ALU, ACT = mybir.AluOpType, mybir.ActivationFunctionType

    ctx = ExitStack()
    with ctx:
        def sb(name, shape, dt=fp32):
            return ctx.enter_context(nc.sbuf_tensor(name, shape, dt))

        def pb(name, shape):
            return ctx.enter_context(nc.psum_tensor(name, shape, fp32))

        def sem(name):
            return ctx.enter_context(nc.semaphore(name))

        adj_raw = sb("adj_raw", [P, RAW_SLOTS, CT * UB])
        adj_hi = sb("adj_hi", [P, HI_SLOTS, CT * UB], fp32r)
        adj_lo = sb("adj_lo", [P, LO_SLOTS, CT * UB], fp32r)
        adj_rest = sb("adj_rest", [P, 2, UB])
        h_hi = sb("h_hi", [P, TILES, HID], fp32r)
        h_lo = sb("h_lo", [P, TILES, HID], fp32r)
        h_rest = sb("h_rest", [P, HID])
        h_full = sb("h_full", [P, 2, HG * HID])
        feat = sb("feat", [P, FEAT_SLOTS, HG * P])
        feat_rest = sb("feat_rest", [P, REST])
        w_item = sb("w_item", [P, HID])
        w_user = sb("w_user", [P, HID])
        bias_item = sb("bias_item", [P, HID])
        bias_user = sb("bias_user", [P, 1])
        identity = sb("identity", [P, P])
        eps = sb("eps", [P, 1])
        x = sb("x", [P, 2, XT * HID])
        stats = sb("stats", [P, XT, 6])
        mean_var = sb("mean_var", [P, XT, 2])
        std = sb("std", [P, XT])
        rstd = sb("rstd", [P, XT])
        neg_mean_rstd = sb("neg_mean_rstd", [P, XT])
        norm = sb("norm", [P, XT * HID])
        norm_t = sb("norm_t", [P, UB])
        relu = sb("relu", [P, UB])
        result = sb("result", [P, 2, UB])

        acc = [pb(f"acc{i}", [P, 512]) for i in range(2)]
        ph = [pb(f"ph{i}", [P, 2, 512]) for i in range(2)]
        px = pb("px", [P, 512])
        pn = pb("pn", [P, 512])

        adj_in = [sem(f"adj_in{s}") for s in range(RAW_SLOTS)]
        rest_in = [sem(f"rest_in{s}") for s in range(2)]
        x_in = [sem(f"x_in{s}") for s in range(2)]
        feat_in = [sem(f"feat_in{s}") for s in range(FEAT_SLOTS)]
        weights_in = sem("weights_in")
        zeroed = sem("zeroed")
        identity_ready = sem("identity_ready")
        hi_ready = sem("hi_ready")
        lo_ready = sem("lo_ready")
        chunk_used = sem("chunk_used")
        h_product = sem("h_product")
        h_summed = sem("h_summed")
        h_hi_ready = sem("h_hi_ready")
        h_lo_ready = sem("h_lo_ready")
        rest_product = sem("rest_product")
        h_rest_ready = sem("h_rest_ready")
        tile_stats = sem("tile_stats")
        moments_ready = sem("moments_ready")
        std_ready = sem("std_ready")
        rstd_ready = sem("rstd_ready")
        scales_ready = sem("scales_ready")
        norm_ready = sem("norm_ready")
        x_transposed = sem("x_transposed")
        norm_transposed = sem("norm_transposed")
        norm_t_ready = sem("norm_t_ready")
        relu_ready = sem("relu_ready")
        result_ready = sem("result_ready")
        stored = sem("stored")

        def uses(b, parity):
            return b * 8 + (16 if parity == 0 else 8)

        def blocks(eng, body):
            body(0, 0)
            body(1, 1)
            with eng.Fori(1, BLOCKS // 2) as pair:
                body(pair * 2, 0)
                body(pair * 2 + 1, 1)

        def known(b, value):
            return isinstance(b, int) and b == value

        def groups_before(c):
            upto = lambda k: min(GROUPS, -(-(CHUNK_AT[k] + CHUNK_TILES[k]) // HG) + 1)
            return range(upto(c - 1) if c else 0, upto(c))

        block = ctx.enter_context(nc.Block())

        @block.sync
        def _(sp):
            def load_group(g):
                if g >= FEAT_SLOTS:
                    sp.wait_ge(h_product, g - FEAT_SLOTS + 1)
                sp.dma_start(feat[:, g % FEAT_SLOTS, :],
                             featt[:, g * HG * P:(g + 1) * HG * P]).then_inc(feat_in[g % FEAT_SLOTS], 16)

            def one_block(b, parity):
                first, second = known(b, 0), known(b, 1)
                for c in range(CHUNKS):
                    if first:
                        for g in groups_before(c):
                            load_group(g)
                        if c == 0:
                            sp.dma_start(w_user[:, :], w_user_t).then_inc(weights_in, 16)
                            sp.dma_start(bias_user[:, :], b_user).then_inc(weights_in, 16)
                            sp.dma_start(feat_rest[:, :], featt[:, TILES * P:ITEMS]).then_inc(weights_in, 16)
                    if not first or c >= RAW_SLOTS:
                        sp.wait_ge(lo_ready, b * CHUNKS + (c - RAW_SLOTS + 1))
                    k, n = CHUNK_AT[c], CHUNK_TILES[c]
                    sp.dma_start(adj_raw[:, c % RAW_SLOTS, 0:n * UB],
                                 adjt[b, :, k * UB:(k + n) * UB]).then_inc(adj_in[c % RAW_SLOTS], 16)
                    if c == 1:
                        if first:
                            sp.wait_ge(zeroed, 1)
                        elif not second:
                            sp.wait_ge(chunk_used, b * CHUNKS - CHUNKS)
                        sp.dma_start(x[:, parity, :], xt[b, :, :]).then_inc(x_in[parity], 16)
                        sp.dma_start(adj_rest[0:REST, parity, :], adjt_rest[b, :, :]).then_inc(rest_in[parity], 16)
                    if c == STORE_BEFORE and not first:
                        sp.wait_ge(result_ready, b)
                        sp.dma_start(out[b - 1, :, :], result[:, 1 - parity, :]).then_inc(stored, 16)

            sp.dma_start(w_item[:, :], w_item_t).then_inc(weights_in, 16)
            sp.dma_start(bias_item[:, :], b_item).then_inc(weights_in, 16)
            blocks(sp, one_block)
            sp.wait_ge(result_ready, BLOCKS)
            sp.dma_start(out[BLOCKS - 1, :, :], result[:, 1, :]).then_inc(stored, 16)
            sp.wait_ge(stored, 16 * BLOCKS)

        @block.gpsimd
        def _(pool):
            nc.gpsimd.memset(h_rest[:, :], 0.0)
            nc.gpsimd.memset(adj_rest[:, :, :], 0.0).then_inc(zeroed, 1)
            nc.gpsimd.memset(eps[:, :], EPS).then_inc(zeroed, 1)
            nc.gpsimd.memset(identity[:, :], 0.0).then_inc(identity_ready, 1)
            pool.wait_ge(identity_ready, 1)
            nc.gpsimd.affine_select(out=identity[:, :], in_=identity[:, :], compare_op=ALU.not_equal, fill=1.0,
                                    base=0, pattern=[[-1, P]], channel_multiplier=1).then_inc(identity_ready, 1)

        @block.scalar
        def _(act):
            def one_block(b, parity):
                first, second = known(b, 0), known(b, 1)
                for c in range(CHUNKS):
                    if first:
                        for g in groups_before(c):
                            act.wait_ge(h_summed, g + 1)
                            nc.scalar.activation(h_hi[:, g * HG:(g + 1) * HG, :], h_full[:, g % 2, :],
                                                 ACT.Copy).then_inc(h_hi_ready, 1)
                    width = CHUNK_TILES[c] * UB
                    act.wait_ge(adj_in[c % RAW_SLOTS], b * (16 * RAW_USES) + 16 * (c // RAW_SLOTS + 1))
                    if not first or c >= HI_SLOTS:
                        act.wait_ge(chunk_used, b * CHUNKS + (c - HI_SLOTS + 1))
                    nc.scalar.activation(adj_hi[:, c % HI_SLOTS, 0:width], adj_raw[:, c % RAW_SLOTS, 0:width],
                                         ACT.Copy).then_inc(hi_ready, 1)
                    if c == RELU_AFTER and not first:
                        finish(b - 1, 1 - parity)
                    if c == STD_AFTER:
                        if first:
                            act.wait_ge(zeroed, 2)
                        act.wait_ge(moments_ready, b + 1)
                        nc.scalar.activation(std[0:UT, :], mean_var[0:UT, :, 1], ACT.Sqrt,
                                             bias=eps[0:UT, :]).then_inc(std_ready, 1)
                    if c == NORM_AFTER:
                        act.wait_ge(scales_ready, b + 1)
                        if not first:
                            act.wait_ge(norm_transposed, b)
                        for t in range(XT):
                            done = nc.scalar.activation(norm[0:UT, t * HID:(t + 1) * HID],
                                                        x[0:UT, parity, t * HID:(t + 1) * HID], ACT.Relu,
                                                        bias=neg_mean_rstd[0:UT, t:t + 1],
                                                        scale=rstd[0:UT, t:t + 1])
                        done.then_inc(norm_ready, 1)

            def finish(b, parity):
                act.wait_ge(chunk_used, (b + 1) * CHUNKS)
                if not known(b, 0):
                    act.wait_ge(result_ready, b)
                nc.scalar.activation(relu[:, :], acc[parity][:, 0:UB], ACT.Relu,
                                     bias=bias_user[:, :]).then_inc(relu_ready, 1)

            act.wait_ge(weights_in, 16 * 5)
            blocks(act, one_block)
            finish(BLOCKS - 1, 1)

        @block.vector
        def _(dve):
            def one_block(b, parity):
                first, second = known(b, 0), known(b, 1)
                for c in range(CHUNKS):
                    if first:
                        for g in groups_before(c):
                            split_h(g)
                        if c == 2:
                            dve.wait_ge(rest_product, 1)
                            dve.wait_ge(zeroed, 1)
                            nc.vector.tensor_tensor(h_rest[0:REST, :], pn[0:REST, 0:HID], bias_item[0:REST, :],
                                                    ALU.add).then_inc(h_rest_ready, 1)
                    width = CHUNK_TILES[c] * UB
                    if c == MOMENTS_AFTER:
                        dve.wait_ge(tile_stats, b + 1)
                    dve.wait_ge(hi_ready, b * CHUNKS + (c + 1))
                    if not first or c >= LO_SLOTS:
                        dve.wait_ge(chunk_used, b * CHUNKS + (c - LO_SLOTS + 1))
                    nc.vector.tensor_tensor(adj_lo[:, c % LO_SLOTS, 0:width], adj_raw[:, c % RAW_SLOTS, 0:width],
                                            adj_hi[:, c % HI_SLOTS, 0:width].bitcast(fp32),
                                            ALU.subtract).then_inc(lo_ready, 1)
                    if c == SUM_AFTER and not first:
                        finish(b - 1, 1 - parity)
                    if c == STATS_AFTER:
                        dve.wait_ge(x_in[parity], uses(b, parity))
                        for t in range(XT):
                            done = nc.vector.bn_stats(stats[0:UT, t, :], x[0:UT, parity, t * HID:(t + 1) * HID])
                        done.then_inc(tile_stats, 1)
                    if c == MOMENTS_AFTER:
                        for t in range(XT):
                            done = nc.vector.bn_aggr(mean_var[0:UT, t, :], stats[0:UT, t, :])
                        done.then_inc(moments_ready, 1)
                    if c == SCALE_AFTER:
                        dve.wait_ge(std_ready, b + 1)
                        if not first:
                            dve.wait_ge(norm_ready, b)
                        nc.vector.reciprocal(rstd[0:UT, :], std[0:UT, :]).then_inc(rstd_ready, 1)
                        dve.wait_ge(rstd_ready, b + 1)
                        nc.vector.scalar_tensor_tensor(out=neg_mean_rstd[0:UT, :], in0=mean_var[0:UT, :, 0],
                                                       scalar=-1.0, in1=rstd[0:UT, :], op0=ALU.mult,
                                                       op1=ALU.mult).then_inc(scales_ready, 1)
                    if c == EVACUATE_AFTER:
                        dve.wait_ge(norm_transposed, b + 1)
                        if not first:
                            dve.wait_ge(chunk_used, b * CHUNKS)
                        nc.vector.tensor_copy(norm_t[:, :], pn[:, 0:UB]).then_inc(norm_t_ready, 1)

            def split_h(g):
                s = g % 2
                dve.wait_ge(h_product, g + 1)
                if g >= 2:
                    dve.wait_ge(h_hi_ready, g - 1)
                    dve.wait_ge(h_lo_ready, g - 1)
                half = HG * HID // 2
                for i in range(2):
                    done = nc.vector.tensor_tensor(
                        h_full[:, s, i * half:(i + 1) * half].rearrange("p (t n) -> p t n", n=HID),
                        ph[s][:, i, 0:half].rearrange("p (t n) -> p t n", n=HID),
                        bias_item[:, :].rearrange("p (t n) -> p t n", t=1).broadcast_to([P, HG // 2, HID]), ALU.add)
                done.then_inc(h_summed, 1)
                dve.wait_ge(h_hi_ready, g + 1)
                nc.vector.tensor_tensor(h_lo[:, g * HG:(g + 1) * HG, :].rearrange("p t n -> p (t n)"), h_full[:, s, :],
                                        h_hi[:, g * HG:(g + 1) * HG, :].rearrange("p t n -> p (t n)").bitcast(fp32),
                                        ALU.subtract).then_inc(h_lo_ready, 1)

            def finish(b, parity):
                dve.wait_ge(relu_ready, b + 1)
                dve.wait_ge(x_transposed, b + 1)
                if not known(b, 0):
                    dve.wait_ge(stored, b * 16)
                nc.vector.tensor_tensor(result[:, parity, :], relu[:, :], px[:, 0:UB],
                                        ALU.add).then_inc(result_ready, 1)

            dve.wait_ge(weights_in, 16 * 5)
            blocks(dve, one_block)
            finish(BLOCKS - 1, 1)

        @block.tensor
        def _(pe):
            def one_block(b, parity):
                first, second = known(b, 0), known(b, 1)
                for c in range(CHUNKS):
                    if first:
                        for g in groups_before(c):
                            pe.wait_ge(feat_in[g % FEAT_SLOTS], 16 * (g // FEAT_SLOTS + 1))
                            if g >= 2:
                                pe.wait_ge(h_summed, g - 1)
                            for t in range(HG):
                                u = t % (HG // 2)
                                done = nc.tensor.matmul(ph[g % 2][:, t // (HG // 2), u * HID:(u + 1) * HID],
                                                        feat[:, g % FEAT_SLOTS, t * P:(t + 1) * P], w_item[:, :],
                                                        start=True, stop=True)
                            done.then_inc(h_product, 1)
                        if c == 0:
                            nc.tensor.matmul(pn[0:REST, 0:HID], feat_rest[:, :], w_item[:, :],
                                             start=True, stop=True).then_inc(rest_product, 1)
                        pe.wait_ge(h_lo_ready, -(-(CHUNK_AT[c] + CHUNK_TILES[c]) // HG))
                    if c == TRANSPOSE_BEFORE:
                        transpose(b, parity, first)
                    if c == EXTRA_BEFORE:
                        pe.wait_ge(rest_in[parity], uses(b, parity))
                        if first:
                            pe.wait_ge(h_rest_ready, 1)
                        nc.tensor.matmul(acc[parity][:, 0:UB], h_rest[:, :], adj_rest[:, parity, :],
                                         start=False, stop=False)
                        pe.wait_ge(norm_t_ready, b + 1)
                        nc.tensor.matmul(acc[parity][:, 0:UB], w_user[:, :], norm_t[:, :], start=False, stop=False)
                    if c == 0 and not first and not second:
                        pe.wait_ge(relu_ready, b - 1)
                    k0, n = CHUNK_AT[c], CHUNK_TILES[c]
                    pe.wait_ge(hi_ready, b * CHUNKS + (c + 1))
                    for t in range(n):
                        moving = adj_hi[:, c % HI_SLOTS, t * UB:(t + 1) * UB]
                        nc.tensor.matmul(acc[parity][:, 0:UB], h_hi[:, k0 + t, :], moving,
                                         start=(c == 0 and t == 0), stop=False)
                        nc.tensor.matmul(acc[parity][:, 0:UB], h_lo[:, k0 + t, :], moving, start=False, stop=False)
                    pe.wait_ge(lo_ready, b * CHUNKS + (c + 1))
                    for t in range(n):
                        end = c == CHUNKS - 1 and t == n - 1
                        done = nc.tensor.matmul(acc[parity][:, 0:UB], h_hi[:, k0 + t, :],
                                                adj_lo[:, c % LO_SLOTS, t * UB:(t + 1) * UB], start=False, stop=end)
                    done.then_inc(chunk_used, 1)

            def transpose(b, parity, first):
                pe.wait_ge(x_in[parity], uses(b, parity))
                if first:
                    pe.wait_ge(identity_ready, 2)
                    pe.wait_ge(h_rest_ready, 1)
                else:
                    pe.wait_ge(result_ready, b)
                for t in range(XT):
                    done = nc.tensor.transpose(px[:, t * UT:(t + 1) * UT], x[0:UT, parity, t * HID:(t + 1) * HID],
                                               identity[0:UT, 0:UT])
                done.then_inc(x_transposed, 1)
                pe.wait_ge(norm_ready, b + 1)
                if not first:
                    pe.wait_ge(norm_t_ready, b)
                for t in range(XT):
                    done = nc.tensor.transpose(pn[:, t * UT:(t + 1) * UT], norm[0:UT, t * HID:(t + 1) * HID],
                                               identity[0:UT, 0:UT])
                done.then_inc(norm_transposed, 1)

            pe.wait_ge(weights_in, 16 * 5)
            blocks(pe, one_block)


def kernel(x, adj, L0_gnn_item_feat, L0_gnn_W_item, L0_gnn_b_item, L0_gnn_W_user, L0_gnn_b_user):
    import numpy as np
    import concourse.bacc as bacc
    from concourse.bass_utils import run_bass_kernel_spmd

    x, adj = np.asarray(x), np.asarray(adj)
    cut = TILES * P
    x_tiles = np.zeros((BLOCKS, P, XT, HID), x.dtype)
    x_tiles[:, 0:UT] = x.reshape(BLOCKS, XT, UT, HID).transpose(0, 2, 1, 3)
    arrays = {
        "adjt": np.ascontiguousarray(adj[:, 0:cut].reshape(BLOCKS, UB, TILES, P).transpose(0, 3, 2, 1))
                  .reshape(BLOCKS, P, TILES * UB),
        "adjt_rest": np.ascontiguousarray(adj[:, cut:].reshape(BLOCKS, UB, REST).transpose(0, 2, 1)),
        "featt": np.ascontiguousarray(np.asarray(L0_gnn_item_feat).T),
        "xt": x_tiles.reshape(BLOCKS, P, XT * HID),
        "w_item_t": np.ascontiguousarray(np.asarray(L0_gnn_W_item).T),
        "w_user_t": np.ascontiguousarray(np.asarray(L0_gnn_W_user).T),
        "b_item": np.ascontiguousarray(np.broadcast_to(np.asarray(L0_gnn_b_item)[None, :], (P, HID))),
        "b_user": np.asarray(L0_gnn_b_user).reshape(HID, 1),
    }
    nc = bacc.Bacc("TRN2", target_bir_lowering=False, num_devices=1)
    args = [nc.dram_tensor(name, a.shape, mybir.dt.from_np(a.dtype), kind="ExternalInput").ap()
            for name, a in arrays.items()]
    out = nc.dram_tensor("out", (BLOCKS, HID, UB), mybir.dt.float32, kind="ExternalOutput").ap()
    gnn_kernel(nc, *args, out)
    r = run_bass_kernel_spmd(nc, [arrays], core_ids=[0])
    return np.ascontiguousarray(r.results[0]["out"].transpose(0, 2, 1)).reshape(USERS, HID)
```

```python
import concourse.bass as bass
from concourse import mybir
from contextlib import ExitStack

USERS, ITEMS, HID = 10000, 10000, 128
P = 128
BLOCKS = 20
UB = USERS // BLOCKS
XT = 4
UT = UB // XT
TILES = ITEMS // P
REST = ITEMS - TILES * P
CHUNKS = 20
CT = -(-TILES // CHUNKS)
CHUNK_TILES = [CT] * (CHUNKS - 1) + [TILES - CT * (CHUNKS - 1)]
CHUNK_AT = [sum(CHUNK_TILES[:c]) for c in range(CHUNKS)]
ROW = 2112
HG = 6
GROUPS = TILES // HG
EPS = 1e-5

RAW_SLOTS, HI_SLOTS, LO_SLOTS, FEAT_SLOTS = 5, 4, 2, 3
RAW_USES = CHUNKS // RAW_SLOTS

REST_HI_HI, REST_LO_HI, REST_HI_LO = 0, 32, 64

GROUP_OF_CHUNK = {4: 0, 7: 1, 10: 2}

RELU_AFTER, SUM_AFTER, STATS_AFTER, MOMENTS_AFTER, STD_AFTER, SCALE_AFTER, NORM_AFTER = 4, 5, 6, 7, 9, 10, 12
REST_AFTER = 3
TRANSPOSE_BEFORE, EVACUATE_AFTER, EXTRA_BEFORE = 14, 16, 19
STORE_BEFORE = 9


def gnn_kernel(nc, adjt, adjt_rest, featt, xt, w_item_t, w_user_t, b_item, b_user, out):
    fp32, fp32r = mybir.dt.float32, mybir.dt.float32r
    ALU, ACT = mybir.AluOpType, mybir.ActivationFunctionType

    ctx = ExitStack()
    with ctx:
        def sb(name, shape, dt=fp32):
            return ctx.enter_context(nc.sbuf_tensor(name, shape, dt))

        def pb(name, shape):
            return ctx.enter_context(nc.psum_tensor(name, shape, fp32))

        def sem(name):
            return ctx.enter_context(nc.semaphore(name))

        adj_raw = sb("adj_raw", [P, RAW_SLOTS, CT * UB])
        adj_hi = sb("adj_hi", [P, HI_SLOTS, CT * UB], fp32r)
        adj_lo = sb("adj_lo", [P, LO_SLOTS, CT * UB], fp32r)
        rest_raw = sb("rest_raw", [P, 2, UB])
        rest_split = sb("rest_split", [P, UB], fp32r)
        h_hi = sb("h_hi", [P, TILES, HID], fp32r)
        h_lo = sb("h_lo", [P, TILES, HID], fp32r)
        h_rest = sb("h_rest", [P, HID])
        h_rest_split = sb("h_rest_split", [P, HID], fp32r)
        h_full = sb("h_full", [P, 2, HG * HID])
        feat = sb("feat", [P, FEAT_SLOTS, HG * P])
        feat_rest = sb("feat_rest", [P, REST])
        w_item = sb("w_item", [P, HID])
        w_user = sb("w_user", [P, HID])
        w_user_hi = sb("w_user_hi", [P, HID], fp32r)
        w_user_lo = sb("w_user_lo", [P, HID], fp32r)
        bias_item = sb("bias_item", [P, HID])
        bias_user = sb("bias_user", [P, 1])
        identity = sb("identity", [P, P])
        eps = sb("eps", [P, 1])
        x = sb("x", [P, 2, XT * HID])
        stats = sb("stats", [P, XT, 6])
        mean_var = sb("mean_var", [P, XT, 2])
        std = sb("std", [P, XT])
        rstd = sb("rstd", [P, XT])
        neg_mean_rstd = sb("neg_mean_rstd", [P, XT])
        norm = sb("norm", [P, XT * HID])
        norm_t_hi = sb("norm_t_hi", [P, UB], fp32r)
        norm_t_lo = sb("norm_t_lo", [P, UB], fp32r)
        relu = sb("relu", [P, UB])
        result = sb("result", [P, 2, UB])

        acc = [pb(f"acc{i}", [P, 512]) for i in range(2)]
        ph = [pb(f"ph{i}", [P, 2, 512]) for i in range(2)]
        px = pb("px", [P, 512])
        pn = pb("pn", [P, 512])

        adj_in = [sem(f"adj_in{s}") for s in range(RAW_SLOTS)]
        rest_in = [sem(f"rest_in{s}") for s in range(2)]
        x_in = [sem(f"x_in{s}") for s in range(2)]
        feat_in = [sem(f"feat_in{s}") for s in range(FEAT_SLOTS)]
        weights_in = sem("weights_in")
        later_weights_in = sem("later_weights_in")
        zeroed = sem("zeroed")
        identity_ready = sem("identity_ready")
        hi_ready = sem("hi_ready")
        lo_ready = sem("lo_ready")
        chunk_used = sem("chunk_used")
        h_product = sem("h_product")
        h_summed = sem("h_summed")
        h_hi_ready = sem("h_hi_ready")
        h_lo_ready = sem("h_lo_ready")
        rest_product = sem("rest_product")
        h_rest_ready = sem("h_rest_ready")
        h_rest_hi_ready = sem("h_rest_hi_ready")
        h_rest_lo_ready = sem("h_rest_lo_ready")
        w_user_hi_ready = sem("w_user_hi_ready")
        w_user_lo_ready = sem("w_user_lo_ready")
        tile_stats = sem("tile_stats")
        moments_ready = sem("moments_ready")
        std_ready = sem("std_ready")
        rstd_ready = sem("rstd_ready")
        scales_ready = sem("scales_ready")
        norm_ready = sem("norm_ready")
        x_transposed = sem("x_transposed")
        norm_transposed = sem("norm_transposed")
        norm_t_hi_ready = sem("norm_t_hi_ready")
        norm_t_lo_ready = sem("norm_t_lo_ready")
        rest_hi_ready = sem("rest_hi_ready")
        rest_lo_ready = sem("rest_lo_ready")
        relu_ready = sem("relu_ready")
        result_ready = sem("result_ready")
        stored = sem("stored")

        def uses(b, parity):
            return b * 8 + (16 if parity == 0 else 8)

        def blocks(eng, body):
            body(0, 0)
            body(1, 1)
            with eng.Fori(1, BLOCKS // 2) as pair:
                body(pair * 2, 0)
                body(pair * 2 + 1, 1)

        def known(b, value):
            return isinstance(b, int) and b == value

        block = ctx.enter_context(nc.Block())

        @block.sync
        def _(sp):
            def load_group(g):
                if g >= FEAT_SLOTS:
                    sp.wait_ge(h_product, g - FEAT_SLOTS + 1)
                sp.dma_start(feat[:, g % FEAT_SLOTS, :],
                             featt[:, g * HG * P:(g + 1) * HG * P]).then_inc(feat_in[g % FEAT_SLOTS], 16)

            def load_chunk(b, c):
                width = CHUNK_TILES[c] * UB
                sp.dma_start(adj_raw[:, c % RAW_SLOTS, 0:width],
                             adjt[b, c, :, 0:width]).then_inc(adj_in[c % RAW_SLOTS], 16)

            def one_block(b, parity):
                first, second = known(b, 0), known(b, 1)
                for c in range(CHUNKS):
                    if not first or c >= RAW_SLOTS:
                        sp.wait_ge(lo_ready, b * CHUNKS + (c - RAW_SLOTS + 1))
                    if not first or c not in GROUP_OF_CHUNK.values():
                        load_chunk(b, c)
                    if c == 1:
                        if not first and not second:
                            sp.wait_ge(chunk_used, b * CHUNKS - CHUNKS)
                        sp.dma_start(x[:, parity, :], xt[b, :, :]).then_inc(x_in[parity], 16)
                        sp.dma_start(rest_raw[0:REST, parity, :], adjt_rest[b, :, :]).then_inc(rest_in[parity], 16)
                    if c == STORE_BEFORE and not first:
                        sp.wait_ge(result_ready, b)
                        sp.dma_start(out[b - 1, :, :], result[:, 1 - parity, :]).then_inc(stored, 16)

            sp.dma_start(w_item[:, :], w_item_t).then_inc(weights_in, 16)
            sp.dma_start(bias_item[:, :], b_item).then_inc(weights_in, 16)
            for g in range(GROUPS):
                load_group(g)
                if g in GROUP_OF_CHUNK:
                    load_chunk(0, GROUP_OF_CHUNK[g])
            sp.dma_start(feat_rest[:, :], featt[:, TILES * P:ITEMS]).then_inc(later_weights_in, 16)
            sp.dma_start(w_user[:, :], w_user_t).then_inc(later_weights_in, 16)
            sp.dma_start(bias_user[:, :], b_user).then_inc(later_weights_in, 16)
            blocks(sp, one_block)
            sp.wait_ge(result_ready, BLOCKS)
            sp.dma_start(out[BLOCKS - 1, :, :], result[:, 1, :]).then_inc(stored, 16)
            sp.wait_ge(stored, 16 * BLOCKS)

        @block.gpsimd
        def _(pool):
            nc.gpsimd.memset(h_rest_split[:, :].bitcast(fp32), 0.0)
            nc.gpsimd.memset(rest_split[:, :].bitcast(fp32), 0.0)
            nc.gpsimd.memset(eps[:, :], EPS).then_inc(zeroed, 1)
            nc.gpsimd.memset(identity[:, :], 0.0).then_inc(identity_ready, 1)
            pool.wait_ge(identity_ready, 1)
            nc.gpsimd.affine_select(out=identity[:, :], in_=identity[:, :], compare_op=ALU.not_equal, fill=1.0,
                                    base=0, pattern=[[-1, P]], channel_multiplier=1).then_inc(identity_ready, 1)

        @block.scalar
        def _(act):
            def one_block(b, parity):
                first, second = known(b, 0), known(b, 1)
                for c in range(CHUNKS):
                    width = CHUNK_TILES[c] * UB
                    act.wait_ge(adj_in[c % RAW_SLOTS], b * (16 * RAW_USES) + 16 * (c // RAW_SLOTS + 1))
                    if not first or c >= HI_SLOTS:
                        act.wait_ge(chunk_used, b * CHUNKS + (c - HI_SLOTS + 1))
                    nc.scalar.activation(adj_hi[:, c % HI_SLOTS, 0:width], adj_raw[:, c % RAW_SLOTS, 0:width],
                                         ACT.Copy).then_inc(hi_ready, 1)
                    if c == RELU_AFTER and not first:
                        finish(b - 1, 1 - parity)
                    if c == REST_AFTER:
                        if first:
                            act.wait_ge(h_rest_ready, 1)
                            act.wait_ge(zeroed, 1)
                            for at in (REST_HI_HI, REST_HI_LO):
                                done = nc.scalar.activation(h_rest_split[at:at + REST, :], h_rest[0:REST, :], ACT.Copy)
                            done.then_inc(h_rest_hi_ready, 1)
                            act.wait_ge(later_weights_in, 16 * 3)
                            nc.scalar.activation(w_user_hi[:, :], w_user[:, :], ACT.Copy).then_inc(w_user_hi_ready, 1)
                        act.wait_ge(rest_in[parity], uses(b, parity))
                        if not first:
                            act.wait_ge(chunk_used, b * CHUNKS)
                        for at in (REST_HI_HI, REST_LO_HI):
                            done = nc.scalar.activation(rest_split[at:at + REST, :], rest_raw[0:REST, parity, :], ACT.Copy)
                        done.then_inc(rest_hi_ready, 1)
                    if c == STD_AFTER:
                        act.wait_ge(moments_ready, b + 1)
                        nc.scalar.activation(std[0:UT, :], mean_var[0:UT, :, 1], ACT.Sqrt,
                                             bias=eps[0:UT, :]).then_inc(std_ready, 1)
                    if c == NORM_AFTER:
                        act.wait_ge(scales_ready, b + 1)
                        if not first:
                            act.wait_ge(norm_transposed, b)
                        for t in range(XT):
                            done = nc.scalar.activation(norm[0:UT, t * HID:(t + 1) * HID],
                                                        x[0:UT, parity, t * HID:(t + 1) * HID], ACT.Relu,
                                                        bias=neg_mean_rstd[0:UT, t:t + 1],
                                                        scale=rstd[0:UT, t:t + 1])
                        done.then_inc(norm_ready, 1)
                    if c == EVACUATE_AFTER:
                        act.wait_ge(norm_transposed, b + 1)
                        if not first:
                            act.wait_ge(chunk_used, b * CHUNKS)
                        nc.scalar.activation(norm_t_hi[:, :], pn[:, 0:UB], ACT.Copy).then_inc(norm_t_hi_ready, 1)

            def finish(b, parity):
                act.wait_ge(chunk_used, (b + 1) * CHUNKS)
                if not known(b, 0):
                    act.wait_ge(result_ready, b)
                nc.scalar.activation(relu[:, :], acc[parity][:, 0:UB], ACT.Relu,
                                     bias=bias_user[:, :]).then_inc(relu_ready, 1)

            for g in range(GROUPS):
                act.wait_ge(h_summed, g + 1)
                nc.scalar.activation(h_hi[:, g * HG:(g + 1) * HG, :], h_full[:, g % 2, :],
                                     ACT.Copy).then_inc(h_hi_ready, 1)
            blocks(act, one_block)
            finish(BLOCKS - 1, 1)

        @block.vector
        def _(dve):
            def one_block(b, parity):
                first, second = known(b, 0), known(b, 1)
                for c in range(CHUNKS):
                    if first and c == 1:
                        dve.wait_ge(rest_product, 1)
                        nc.vector.tensor_tensor(h_rest[0:REST, :], pn[0:REST, 0:HID], bias_item[0:REST, :],
                                                ALU.add).then_inc(h_rest_ready, 1)
                    width = CHUNK_TILES[c] * UB
                    if c == MOMENTS_AFTER:
                        dve.wait_ge(tile_stats, b + 1)
                    dve.wait_ge(hi_ready, b * CHUNKS + (c + 1))
                    if not first or c >= LO_SLOTS:
                        dve.wait_ge(chunk_used, b * CHUNKS + (c - LO_SLOTS + 1))
                    nc.vector.tensor_tensor(adj_lo[:, c % LO_SLOTS, 0:width], adj_raw[:, c % RAW_SLOTS, 0:width],
                                            adj_hi[:, c % HI_SLOTS, 0:width].bitcast(fp32),
                                            ALU.subtract).then_inc(lo_ready, 1)
                    if c == SUM_AFTER and not first:
                        finish(b - 1, 1 - parity)
                    if c == STATS_AFTER:
                        dve.wait_ge(x_in[parity], uses(b, parity))
                        for t in range(XT):
                            done = nc.vector.bn_stats(stats[0:UT, t, :], x[0:UT, parity, t * HID:(t + 1) * HID])
                        done.then_inc(tile_stats, 1)
                    if c == MOMENTS_AFTER:
                        for t in range(XT):
                            done = nc.vector.bn_aggr(mean_var[0:UT, t, :], stats[0:UT, t, :])
                        done.then_inc(moments_ready, 1)
                    if c == SCALE_AFTER:
                        dve.wait_ge(std_ready, b + 1)
                        if not first:
                            dve.wait_ge(norm_ready, b)
                        nc.vector.reciprocal(rstd[0:UT, :], std[0:UT, :]).then_inc(rstd_ready, 1)
                        dve.wait_ge(rstd_ready, b + 1)
                        nc.vector.scalar_tensor_tensor(out=neg_mean_rstd[0:UT, :], in0=mean_var[0:UT, :, 0],
                                                       scalar=-1.0, in1=rstd[0:UT, :], op0=ALU.mult,
                                                       op1=ALU.mult).then_inc(scales_ready, 1)
                    if c == REST_AFTER + 1:
                        if first:
                            dve.wait_ge(h_rest_hi_ready, 1)
                            nc.vector.tensor_tensor(h_rest_split[REST_LO_HI:REST_LO_HI + REST, :], h_rest[0:REST, :],
                                                    h_rest_split[REST_HI_HI:REST_HI_HI + REST, :].bitcast(fp32),
                                                    ALU.subtract).then_inc(h_rest_lo_ready, 1)
                            dve.wait_ge(w_user_hi_ready, 1)
                            nc.vector.tensor_tensor(w_user_lo[:, :], w_user[:, :], w_user_hi[:, :].bitcast(fp32),
                                                    ALU.subtract).then_inc(w_user_lo_ready, 1)
                        dve.wait_ge(rest_hi_ready, b + 1)
                        nc.vector.tensor_tensor(rest_split[REST_HI_LO:REST_HI_LO + REST, :], rest_raw[0:REST, parity, :],
                                                rest_split[REST_HI_HI:REST_HI_HI + REST, :].bitcast(fp32),
                                                ALU.subtract).then_inc(rest_lo_ready, 1)
                    if c == EVACUATE_AFTER + 1:
                        dve.wait_ge(norm_t_hi_ready, b + 1)
                        nc.vector.tensor_tensor(norm_t_lo[:, :], pn[:, 0:UB], norm_t_hi[:, :].bitcast(fp32),
                                                ALU.subtract).then_inc(norm_t_lo_ready, 1)

            def sum_h(g):
                dve.wait_ge(h_product, g + 1)
                if g >= 2:
                    dve.wait_ge(h_hi_ready, g - 1)
                    dve.wait_ge(h_lo_ready, g - 1)
                half = HG * HID // 2
                for i in range(2):
                    done = nc.vector.tensor_tensor(
                        h_full[:, g % 2, i * half:(i + 1) * half].rearrange("p (t n) -> p t n", n=HID),
                        ph[g % 2][:, i, 0:half].rearrange("p (t n) -> p t n", n=HID),
                        bias_item[:, :].rearrange("p (t n) -> p t n", t=1).broadcast_to([P, HG // 2, HID]), ALU.add)
                done.then_inc(h_summed, 1)

            def rest_of_h(g):
                dve.wait_ge(h_hi_ready, g + 1)
                nc.vector.tensor_tensor(h_lo[:, g * HG:(g + 1) * HG, :].rearrange("p t n -> p (t n)"), h_full[:, g % 2, :],
                                        h_hi[:, g * HG:(g + 1) * HG, :].rearrange("p t n -> p (t n)").bitcast(fp32),
                                        ALU.subtract).then_inc(h_lo_ready, 1)

            def finish(b, parity):
                dve.wait_ge(relu_ready, b + 1)
                dve.wait_ge(x_transposed, b + 1)
                if not known(b, 0):
                    dve.wait_ge(stored, b * 16)
                nc.vector.tensor_tensor(result[:, parity, :], relu[:, :], px[:, 0:UB],
                                        ALU.add).then_inc(result_ready, 1)

            dve.wait_ge(weights_in, 16 * 2)
            sum_h(0)
            for g in range(1, GROUPS):
                sum_h(g)
                rest_of_h(g - 1)
            rest_of_h(GROUPS - 1)
            blocks(dve, one_block)
            finish(BLOCKS - 1, 1)

        @block.tensor
        def _(pe):
            def one_block(b, parity):
                first, second = known(b, 0), known(b, 1)
                for c in range(CHUNKS):
                    if c == TRANSPOSE_BEFORE:
                        transpose(b, parity, first)
                    if c == EXTRA_BEFORE:
                        pe.wait_ge(rest_lo_ready, b + 1)
                        if first:
                            pe.wait_ge(h_rest_lo_ready, 1)
                            pe.wait_ge(w_user_lo_ready, 1)
                        into = acc[parity][:, 0:UB]
                        nc.tensor.matmul(into, h_rest_split[:, :], rest_split[:, :], start=False, stop=False)
                        pe.wait_ge(norm_t_lo_ready, b + 1)
                        nc.tensor.matmul(into, w_user_hi[:, :], norm_t_hi[:, :], start=False, stop=False)
                        nc.tensor.matmul(into, w_user_lo[:, :], norm_t_hi[:, :], start=False, stop=False)
                        nc.tensor.matmul(into, w_user_hi[:, :], norm_t_lo[:, :], start=False, stop=False)
                    if c == 0 and not first and not second:
                        pe.wait_ge(relu_ready, b - 1)
                    k0, n = CHUNK_AT[c], CHUNK_TILES[c]
                    pe.wait_ge(hi_ready, b * CHUNKS + (c + 1))
                    for t in range(n):
                        moving = adj_hi[:, c % HI_SLOTS, t * UB:(t + 1) * UB]
                        nc.tensor.matmul(acc[parity][:, 0:UB], h_hi[:, k0 + t, :], moving,
                                         start=(c == 0 and t == 0), stop=False)
                        nc.tensor.matmul(acc[parity][:, 0:UB], h_lo[:, k0 + t, :], moving, start=False, stop=False)
                    pe.wait_ge(lo_ready, b * CHUNKS + (c + 1))
                    for t in range(n):
                        end = c == CHUNKS - 1 and t == n - 1
                        done = nc.tensor.matmul(acc[parity][:, 0:UB], h_hi[:, k0 + t, :],
                                                adj_lo[:, c % LO_SLOTS, t * UB:(t + 1) * UB], start=False, stop=end)
                    done.then_inc(chunk_used, 1)

            def transpose(b, parity, first):
                pe.wait_ge(x_in[parity], uses(b, parity))
                if first:
                    pe.wait_ge(identity_ready, 2)
                    pe.wait_ge(h_rest_ready, 1)
                else:
                    pe.wait_ge(result_ready, b)
                for t in range(XT):
                    done = nc.tensor.transpose(px[:, t * UT:(t + 1) * UT], x[0:UT, parity, t * HID:(t + 1) * HID],
                                               identity[0:UT, 0:UT])
                done.then_inc(x_transposed, 1)
                pe.wait_ge(norm_ready, b + 1)
                if not first:
                    pe.wait_ge(norm_t_lo_ready, b)
                for t in range(XT):
                    done = nc.tensor.transpose(pn[:, t * UT:(t + 1) * UT], norm[0:UT, t * HID:(t + 1) * HID],
                                               identity[0:UT, 0:UT])
                done.then_inc(norm_transposed, 1)

            pe.wait_ge(weights_in, 16 * 2)
            for g in range(GROUPS):
                pe.wait_ge(feat_in[g % FEAT_SLOTS], 16 * (g // FEAT_SLOTS + 1))
                if g >= 2:
                    pe.wait_ge(h_summed, g - 1)
                for t in range(HG):
                    u = t % (HG // 2)
                    done = nc.tensor.matmul(ph[g % 2][:, t // (HG // 2), u * HID:(u + 1) * HID],
                                            feat[:, g % FEAT_SLOTS, t * P:(t + 1) * P], w_item[:, :],
                                            start=True, stop=True)
                done.then_inc(h_product, 1)
            pe.wait_ge(later_weights_in, 16 * 3)
            nc.tensor.matmul(pn[0:REST, 0:HID], feat_rest[:, :], w_item[:, :], start=True, stop=True).then_inc(rest_product, 1)
            pe.wait_ge(h_lo_ready, GROUPS)
            blocks(pe, one_block)


def kernel(x, adj, L0_gnn_item_feat, L0_gnn_W_item, L0_gnn_b_item, L0_gnn_W_user, L0_gnn_b_user):
    import numpy as np
    import concourse.bacc as bacc
    from concourse.bass_utils import run_bass_kernel_spmd

    x, adj = np.asarray(x), np.asarray(adj)
    cut = TILES * P
    x_tiles = np.zeros((BLOCKS, P, XT, HID), x.dtype)
    x_tiles[:, 0:UT] = x.reshape(BLOCKS, XT, UT, HID).transpose(0, 2, 1, 3)
    tiles = adj[:, 0:cut].reshape(BLOCKS, UB, TILES, P)
    adjt = np.zeros((BLOCKS, CHUNKS, P, ROW), adj.dtype)
    for c, (k, n) in enumerate(zip(CHUNK_AT, CHUNK_TILES)):
        adjt[:, c, :, 0:n * UB].reshape(BLOCKS, P, n, UB)[...] = tiles[:, :, k:k + n].transpose(0, 3, 2, 1)
    arrays = {
        "adjt": adjt,
        "adjt_rest": np.ascontiguousarray(adj[:, cut:].reshape(BLOCKS, UB, REST).transpose(0, 2, 1)),
        "featt": np.ascontiguousarray(np.asarray(L0_gnn_item_feat).T),
        "xt": x_tiles.reshape(BLOCKS, P, XT * HID),
        "w_item_t": np.ascontiguousarray(np.asarray(L0_gnn_W_item).T),
        "w_user_t": np.ascontiguousarray(np.asarray(L0_gnn_W_user).T),
        "b_item": np.ascontiguousarray(np.broadcast_to(np.asarray(L0_gnn_b_item)[None, :], (P, HID))),
        "b_user": np.asarray(L0_gnn_b_user).reshape(HID, 1),
    }
    nc = bacc.Bacc("TRN2", target_bir_lowering=False, num_devices=1)
    args = [nc.dram_tensor(name, a.shape, mybir.dt.from_np(a.dtype), kind="ExternalInput").ap()
            for name, a in arrays.items()]
    out = nc.dram_tensor("out", (BLOCKS, HID, UB), mybir.dt.float32, kind="ExternalOutput").ap()
    gnn_kernel(nc, *args, out)
    r = run_bass_kernel_spmd(nc, [arrays], core_ids=[0])
    return np.ascontiguousarray(r.results[0]["out"].transpose(0, 2, 1)).reshape(USERS, HID)
```

```python
import concourse.bass as bass
from concourse import mybir
from contextlib import ExitStack

USERS, ITEMS, HID = 10000, 10000, 128
P = 128
BLOCKS = 20
UB = USERS // BLOCKS
XT = 4
UT = UB // XT
TILES = ITEMS // P
REST = ITEMS - TILES * P
CHUNKS = 20
CT = -(-TILES // CHUNKS)
CUT = [CT] * (CHUNKS - 1) + [TILES - CT * (CHUNKS - 1)]
LAST_CUT = CUT[:-6] + [2] * 10 + [1, 1]
ROW = 2112
HG = 6
GROUPS = TILES // HG
BANK_TILES = HG // 2
BIAS_HI, BIAS_LO = 0, 32
EPS = 1e-5
HALVES = [(0, UB // 2), (UB // 2, UB)]

RAW_SLOTS, HI_SLOTS, LO_SLOTS, FEAT_SLOTS = 5, 4, 2, 5
RAW_USES = CHUNKS // RAW_SLOTS

REST_HI_HI, REST_LO_HI, REST_HI_LO = 0, 32, 64

CHUNK_BEHIND_GROUP = {4: 0, 5: 1, 9: 2}

EARLY_CHUNKS = 2
EARLY_GROUP = GROUPS - EARLY_CHUNKS * CT

RELU_AFTER, SUM_AFTER, STATS_AFTER, MOMENTS_AFTER, STD_AFTER, SCALE_AFTER, NORM_AFTER = 4, 5, 2, 3, 5, 6, 8
REST_AFTER, TRANSPOSE_BEFORE, EVACUATE_AFTER, EXTRA_BEFORE = 9, 10, 12, 15
STORE_BEFORE = 9


def gnn_kernel(nc, adjt, adjt_rest, featt, xt, w_item_t, w_user_t, b_item, b_user, out):
    fp32, fp32r = mybir.dt.float32, mybir.dt.float32r
    ALU, ACT = mybir.AluOpType, mybir.ActivationFunctionType

    ctx = ExitStack()
    with ctx:
        def sb(name, shape, dt=fp32):
            return ctx.enter_context(nc.sbuf_tensor(name, shape, dt))

        def pb(name, shape):
            return ctx.enter_context(nc.psum_tensor(name, shape, fp32))

        def sem(name):
            return ctx.enter_context(nc.semaphore(name))

        adj_raw = sb("adj_raw", [P, RAW_SLOTS, CT * UB])
        adj_hi = sb("adj_hi", [P, HI_SLOTS, CT * UB], fp32r)
        adj_lo = sb("adj_lo", [P, LO_SLOTS, CT * UB], fp32r)
        rest_raw = sb("rest_raw", [P, 2, UB])
        rest_split = sb("rest_split", [P, UB], fp32r)
        h_hi = sb("h_hi", [P, TILES, HID], fp32r)
        h_lo = sb("h_lo", [P, TILES, HID], fp32r)
        h_rest = sb("h_rest", [P, HID])
        h_rest_split = sb("h_rest_split", [P, HID], fp32r)
        feat = sb("feat", [P, FEAT_SLOTS, HG * P])
        feat_rest = sb("feat_rest", [P, REST])
        w_item = sb("w_item", [P, HID])
        w_user = sb("w_user", [P, HID])
        w_user_hi = sb("w_user_hi", [P, HID], fp32r)
        w_user_lo = sb("w_user_lo", [P, HID], fp32r)
        ones = sb("ones", [P, P], fp32r)
        bias_item = sb("bias_item", [1, BANK_TILES * HID])
        bias_split = sb("bias_split", [P, BANK_TILES * HID], fp32r)
        bias_user = sb("bias_user", [P, 1])
        identity = sb("identity", [P, P])
        eps = sb("eps", [P, 1])
        x = sb("x", [P, 2, XT * HID])
        stats = sb("stats", [P, XT, 6])
        mean_var = sb("mean_var", [P, XT, 2])
        std = sb("std", [P, XT])
        var_eps = sb("var_eps", [P, XT])
        rough = sb("rough", [P, XT])
        newton = sb("newton", [P, 2, XT])
        rstd = sb("rstd", [P, XT])
        neg_mean_rstd = sb("neg_mean_rstd", [P, XT])
        norm = sb("norm", [P, XT * HID])
        norm_t_hi = sb("norm_t_hi", [P, UB], fp32r)
        norm_t_lo = sb("norm_t_lo", [P, UB], fp32r)
        result = sb("result", [P, 2, UB])

        acc = [pb(f"acc{i}", [P, 512]) for i in range(2)]
        ph = [pb(f"ph{i}", [P, 2, 512]) for i in range(2)]
        px = pb("px", [P, 512])
        pn = pb("pn", [P, 512])

        adj_in = [sem(f"adj_in{s}") for s in range(RAW_SLOTS)]
        rest_in = [sem(f"rest_in{s}") for s in range(2)]
        x_in = [sem(f"x_in{s}") for s in range(2)]
        feat_in = [sem(f"feat_in{s}") for s in range(FEAT_SLOTS)]
        bias_in = sem("bias_in")
        weights_in = sem("weights_in")
        later_weights_in = sem("later_weights_in")
        bias_zeroed = sem("bias_zeroed")
        zeroed = sem("zeroed")
        identity_ready = sem("identity_ready")
        hi_ready = sem("hi_ready")
        early_hi_ready = sem("early_hi_ready")
        lo_ready = sem("lo_ready")
        chunk_used = sem("chunk_used")
        bias_hi_ready = sem("bias_hi_ready")
        bias_lo_ready = sem("bias_lo_ready")
        h_product = sem("h_product")
        h_hi_ready = sem("h_hi_ready")
        h_lo_ready = sem("h_lo_ready")
        rest_product = sem("rest_product")
        h_rest_ready = sem("h_rest_ready")
        h_rest_hi_ready = sem("h_rest_hi_ready")
        h_rest_lo_ready = sem("h_rest_lo_ready")
        w_user_hi_ready = sem("w_user_hi_ready")
        w_user_lo_ready = sem("w_user_lo_ready")
        tile_stats = sem("tile_stats")
        moments_ready = sem("moments_ready")
        std_ready = sem("std_ready")
        newton_steps = sem("newton_steps")
        rstd_ready = sem("rstd_ready")
        scales_ready = sem("scales_ready")
        norm_ready = sem("norm_ready")
        x_transposed = sem("x_transposed")
        norm_transposed = sem("norm_transposed")
        norm_t_hi_ready = sem("norm_t_hi_ready")
        norm_t_lo_ready = sem("norm_t_lo_ready")
        rest_hi_ready = sem("rest_hi_ready")
        rest_lo_ready = sem("rest_lo_ready")
        relu_ready = sem("relu_ready")
        result_ready = sem("result_ready")
        stored = sem("stored")

        def uses(b, parity):
            return b * 8 + (16 if parity == 0 else 8)

        def blocks(eng, body):
            body(0, 0, CUT)
            body(1, 1, CUT)
            with eng.Fori(1, BLOCKS // 2 - 1) as pair:
                body(pair * 2, 0, CUT)
                body(pair * 2 + 1, 1, CUT)
            body(BLOCKS - 2, 0, CUT)
            body(BLOCKS - 1, 1, LAST_CUT)

        def known(b, value):
            return isinstance(b, int) and b == value

        def of_group(h, g):
            return h[:, g * HG:(g + 1) * HG, :].rearrange("p (i t) n -> p i (t n)", i=2)

        block = ctx.enter_context(nc.Block())

        @block.sync
        def _(sp):
            def load_group(g):
                if g >= FEAT_SLOTS:
                    sp.wait_ge(h_product, g - FEAT_SLOTS + 1)
                sp.dma_start(feat[:, g % FEAT_SLOTS, :],
                             featt[:, g * HG * P:(g + 1) * HG * P]).then_inc(feat_in[g % FEAT_SLOTS], 16)

            def load_chunk(b, c, cut):
                k, width = sum(cut[:c]), cut[c] * UB
                sp.dma_start(adj_raw[:, c % RAW_SLOTS, 0:width],
                             adjt[b, k // CT, :, k % CT * UB:k % CT * UB + width]).then_inc(adj_in[c % RAW_SLOTS], 16)

            def one_block(b, parity, cut):
                first, second = known(b, 0), known(b, 1)
                for c, n in enumerate(cut):
                    if not first or c >= RAW_SLOTS:
                        sp.wait_ge(lo_ready, b * CHUNKS + (c - RAW_SLOTS + 1))
                    if not first or c not in CHUNK_BEHIND_GROUP.values():
                        load_chunk(b, c, cut)
                    if c == 1:
                        if not first and not second:
                            sp.wait_ge(chunk_used, b * CHUNKS - CHUNKS)
                        sp.dma_start(x[:, parity, :], xt[b, :, :]).then_inc(x_in[parity], 16)
                        sp.dma_start(rest_raw[0:REST, parity, :], adjt_rest[b, :, :]).then_inc(rest_in[parity], 16)
                    if c == STORE_BEFORE and not first:
                        sp.wait_ge(result_ready, b)
                        sp.dma_start(out[b - 1, :, :], result[:, 1 - parity, :]).then_inc(stored, 16)

            load_group(0)
            sp.dma_start(bias_item[:, :], b_item).then_inc(bias_in, 16)
            sp.dma_start(w_item[:, :], w_item_t).then_inc(weights_in, 16)
            for g in range(1, GROUPS):
                load_group(g)
                if g in CHUNK_BEHIND_GROUP:
                    load_chunk(0, CHUNK_BEHIND_GROUP[g], CUT)
            sp.dma_start(feat_rest[:, :], featt[:, TILES * P:ITEMS]).then_inc(later_weights_in, 16)
            sp.dma_start(w_user[:, :], w_user_t).then_inc(later_weights_in, 16)
            sp.dma_start(bias_user[:, :], b_user).then_inc(later_weights_in, 16)
            blocks(sp, one_block)
            for i, (at, end) in enumerate(HALVES):
                sp.wait_ge(result_ready, BLOCKS + i)
                sp.dma_start(out[BLOCKS - 1, :, at:end], result[:, 1, at:end]).then_inc(stored, 16)
            sp.wait_ge(stored, 16 * (BLOCKS - 1 + len(HALVES)))

        @block.gpsimd
        def _(pool):
            nc.gpsimd.memset(bias_split[:, :].bitcast(fp32), 0.0).then_inc(bias_zeroed, 1)
            nc.gpsimd.memset(ones[:, :].bitcast(fp32), 1.0).then_inc(bias_zeroed, 1)
            nc.gpsimd.memset(h_rest_split[:, :].bitcast(fp32), 0.0).then_inc(zeroed, 1)
            nc.gpsimd.memset(rest_split[:, :].bitcast(fp32), 0.0).then_inc(zeroed, 1)
            nc.gpsimd.memset(eps[:, :], EPS).then_inc(zeroed, 1)
            nc.gpsimd.memset(identity[:, :], 0.0).then_inc(identity_ready, 1)
            pool.wait_ge(identity_ready, 1)
            nc.gpsimd.affine_select(out=identity[:, :], in_=identity[:, :], compare_op=ALU.not_equal, fill=1.0,
                                    base=0, pattern=[[-1, P]], channel_multiplier=1).then_inc(identity_ready, 1)

        @block.scalar
        def _(act):
            def round_adj(c, at, end):
                return nc.scalar.activation(adj_hi[:, c % HI_SLOTS, at:end], adj_raw[:, c % RAW_SLOTS, at:end], ACT.Copy)

            def one_block(b, parity, cut):
                first = known(b, 0)
                for c, n in enumerate(cut):
                    if not first or c >= EARLY_CHUNKS:
                        act.wait_ge(adj_in[c % RAW_SLOTS], b * (16 * RAW_USES) + 16 * (c // RAW_SLOTS + 1))
                        if not first or c >= HI_SLOTS:
                            act.wait_ge(chunk_used, b * CHUNKS + (c - HI_SLOTS + 1))
                        round_adj(c, 0, n * UB).then_inc(hi_ready, 1)
                    if c == RELU_AFTER and not first:
                        finish(b - 1, 1 - parity, b * CHUNKS)
                    if c == REST_AFTER:
                        if first:
                            act.wait_ge(h_rest_ready, 1)
                            act.wait_ge(zeroed, 3)
                            for at in (REST_HI_HI, REST_HI_LO):
                                done = nc.scalar.activation(h_rest_split[at:at + REST, :], h_rest[0:REST, :], ACT.Copy)
                            done.then_inc(h_rest_hi_ready, 1)
                            act.wait_ge(later_weights_in, 16 * 3)
                            nc.scalar.activation(w_user_hi[:, :], w_user[:, :], ACT.Copy).then_inc(w_user_hi_ready, 1)
                        act.wait_ge(rest_in[parity], uses(b, parity))
                        if not first:
                            act.wait_ge(chunk_used, b * CHUNKS)
                        for at in (REST_HI_HI, REST_LO_HI):
                            done = nc.scalar.activation(rest_split[at:at + REST, :], rest_raw[0:REST, parity, :], ACT.Copy)
                        done.then_inc(rest_hi_ready, 1)
                    if c == STD_AFTER:
                        if first:
                            act.wait_ge(zeroed, 3)
                        act.wait_ge(moments_ready, b + 1)
                        nc.scalar.activation(std[0:UT, :], mean_var[0:UT, :, 1], ACT.Sqrt,
                                             bias=eps[0:UT, :]).then_inc(std_ready, 1)
                    if c == NORM_AFTER:
                        act.wait_ge(scales_ready, b + 1)
                        if not first:
                            act.wait_ge(norm_transposed, b)
                        for t in range(XT):
                            done = nc.scalar.activation(norm[0:UT, t * HID:(t + 1) * HID],
                                                        x[0:UT, parity, t * HID:(t + 1) * HID], ACT.Relu,
                                                        bias=neg_mean_rstd[0:UT, t:t + 1],
                                                        scale=rstd[0:UT, t:t + 1])
                        done.then_inc(norm_ready, 1)
                    if c == EVACUATE_AFTER:
                        act.wait_ge(norm_transposed, b + 1)
                        if not first:
                            act.wait_ge(chunk_used, b * CHUNKS)
                        nc.scalar.activation(norm_t_hi[:, :], pn[:, 0:UB], ACT.Copy).then_inc(norm_t_hi_ready, 1)

            def finish(b, parity, chunks):
                act.wait_ge(chunk_used, chunks)
                if not known(b, 0):
                    act.wait_ge(stored, b * 16)
                for at, end in HALVES if known(b, BLOCKS - 1) else [(0, UB)]:
                    nc.scalar.activation(result[:, parity, at:end], acc[parity][:, at:end], ACT.Relu,
                                         bias=bias_user[:, :]).then_inc(relu_ready, 1)

            act.wait_ge(bias_in, 16)
            act.wait_ge(bias_zeroed, 2)
            nc.scalar.activation(bias_split[BIAS_HI:BIAS_HI + 1, :], bias_item[:, :], ACT.Copy).then_inc(bias_hi_ready, 1)
            for g in range(GROUPS):
                act.wait_ge(h_product, g + 1)
                nc.scalar.activation(of_group(h_hi, g), ph[g % 2][:, :, 0:BANK_TILES * HID], ACT.Copy).then_inc(h_hi_ready, 1)
                if g >= EARLY_GROUP:
                    c, t = (g - EARLY_GROUP) // CT, (g - EARLY_GROUP) % CT
                    if t == 0:
                        act.wait_ge(adj_in[c], 16)
                    round_adj(c, t * UB, (t + 1) * UB).then_inc(early_hi_ready if t < CT - 1 else hi_ready, 1)
            blocks(act, one_block)
            finish(BLOCKS - 1, 1, BLOCKS * CHUNKS + len(LAST_CUT) - len(CUT))

        @block.vector
        def _(dve):
            def rest_of_adj(c, at, end):
                return nc.vector.tensor_tensor(adj_lo[:, c % LO_SLOTS, at:end], adj_raw[:, c % RAW_SLOTS, at:end],
                                               adj_hi[:, c % HI_SLOTS, at:end].bitcast(fp32), ALU.subtract)

            def one_block(b, parity, cut):
                first = known(b, 0)
                for c, n in enumerate(cut):
                    if first and c == 1:
                        dve.wait_ge(rest_product, 1)
                        nc.vector.tensor_copy(h_rest[0:REST, :], pn[0:REST, 0:HID]).then_inc(h_rest_ready, 1)
                    if c == MOMENTS_AFTER:
                        dve.wait_ge(tile_stats, b + 1)
                    if not first or c >= EARLY_CHUNKS:
                        dve.wait_ge(hi_ready, b * CHUNKS + (c + 1))
                        if not first or c >= LO_SLOTS:
                            dve.wait_ge(chunk_used, b * CHUNKS + (c - LO_SLOTS + 1))
                        rest_of_adj(c, 0, n * UB).then_inc(lo_ready, 1)
                    if c == SUM_AFTER and not first:
                        finish(b - 1, 1 - parity)
                    if c == STATS_AFTER:
                        dve.wait_ge(x_in[parity], uses(b, parity))
                        for t in range(XT):
                            done = nc.vector.bn_stats(stats[0:UT, t, :], x[0:UT, parity, t * HID:(t + 1) * HID])
                        done.then_inc(tile_stats, 1)
                    if c == MOMENTS_AFTER:
                        for t in range(XT):
                            done = nc.vector.bn_aggr(mean_var[0:UT, t, :], stats[0:UT, t, :])
                        done.then_inc(moments_ready, 1)
                    if c == SCALE_AFTER:
                        dve.wait_ge(std_ready, b + 1)
                        if not first:
                            dve.wait_ge(norm_ready, b)
                        nc.vector.tensor_scalar(var_eps[0:UT, :], mean_var[0:UT, :, 1], EPS, None,
                                                ALU.add).then_inc(newton_steps, 1)
                        nc.vector.reciprocal(rough[0:UT, :], std[0:UT, :]).then_inc(newton_steps, 1)
                        dve.wait_ge(newton_steps, b * 4 + 2)
                        nc.vector.scalar_tensor_tensor(out=newton[0:UT, 0, :], in0=rough[0:UT, :], scalar=-0.5,
                                                       in1=rough[0:UT, :], op0=ALU.mult,
                                                       op1=ALU.mult).then_inc(newton_steps, 1)
                        dve.wait_ge(newton_steps, b * 4 + 3)
                        nc.vector.tensor_tensor(newton[0:UT, 1, :], newton[0:UT, 0, :], var_eps[0:UT, :],
                                                ALU.mult).then_inc(newton_steps, 1)
                        dve.wait_ge(newton_steps, b * 4 + 4)
                        nc.vector.scalar_tensor_tensor(out=rstd[0:UT, :], in0=newton[0:UT, 1, :], scalar=1.5,
                                                       in1=rough[0:UT, :], op0=ALU.add,
                                                       op1=ALU.mult).then_inc(rstd_ready, 1)
                        dve.wait_ge(rstd_ready, b + 1)
                        nc.vector.scalar_tensor_tensor(out=neg_mean_rstd[0:UT, :], in0=mean_var[0:UT, :, 0],
                                                       scalar=-1.0, in1=rstd[0:UT, :], op0=ALU.mult,
                                                       op1=ALU.mult).then_inc(scales_ready, 1)
                    if c == REST_AFTER + 1:
                        if first:
                            dve.wait_ge(h_rest_hi_ready, 1)
                            nc.vector.tensor_tensor(h_rest_split[REST_LO_HI:REST_LO_HI + REST, :], h_rest[0:REST, :],
                                                    h_rest_split[REST_HI_HI:REST_HI_HI + REST, :].bitcast(fp32),
                                                    ALU.subtract).then_inc(h_rest_lo_ready, 1)
                            dve.wait_ge(w_user_hi_ready, 1)
                            nc.vector.tensor_tensor(w_user_lo[:, :], w_user[:, :], w_user_hi[:, :].bitcast(fp32),
                                                    ALU.subtract).then_inc(w_user_lo_ready, 1)
                        dve.wait_ge(rest_hi_ready, b + 1)
                        nc.vector.tensor_tensor(rest_split[REST_HI_LO:REST_HI_LO + REST, :], rest_raw[0:REST, parity, :],
                                                rest_split[REST_HI_HI:REST_HI_HI + REST, :].bitcast(fp32),
                                                ALU.subtract).then_inc(rest_lo_ready, 1)
                    if c == EVACUATE_AFTER + 1:
                        dve.wait_ge(norm_t_hi_ready, b + 1)
                        nc.vector.tensor_tensor(norm_t_lo[:, :], pn[:, 0:UB], norm_t_hi[:, :].bitcast(fp32),
                                                ALU.subtract).then_inc(norm_t_lo_ready, 1)

            def finish(b, parity):
                dve.wait_ge(x_transposed, b + 1)
                for i, (at, end) in enumerate(HALVES if known(b, BLOCKS - 1) else [(0, UB)]):
                    dve.wait_ge(relu_ready, b + (1 + i))
                    nc.vector.tensor_tensor(result[:, parity, at:end], result[:, parity, at:end], px[:, at:end],
                                            ALU.add).then_inc(result_ready, 1)

            dve.wait_ge(bias_hi_ready, 1)
            nc.vector.tensor_tensor(bias_split[BIAS_LO:BIAS_LO + 1, :], bias_item[:, :],
                                    bias_split[BIAS_HI:BIAS_HI + 1, :].bitcast(fp32), ALU.subtract).then_inc(bias_lo_ready, 1)
            for g in range(GROUPS):
                dve.wait_ge(h_hi_ready, g + 1)
                nc.vector.tensor_tensor(of_group(h_lo, g), ph[g % 2][:, :, 0:BANK_TILES * HID],
                                        of_group(h_hi, g).bitcast(fp32), ALU.subtract).then_inc(h_lo_ready, 1)
                if g >= EARLY_GROUP:
                    c, t = (g - EARLY_GROUP) // CT, (g - EARLY_GROUP) % CT
                    if t < CT - 1:
                        dve.wait_ge(early_hi_ready, c * (CT - 1) + t + 1)
                    else:
                        dve.wait_ge(hi_ready, c + 1)
                    done = rest_of_adj(c, t * UB, (t + 1) * UB)
                    if t == CT - 1:
                        done.then_inc(lo_ready, 1)
            blocks(dve, one_block)
            finish(BLOCKS - 1, 1)

        @block.tensor
        def _(pe):
            def one_block(b, parity, cut):
                first, second = known(b, 0), known(b, 1)
                for c, n in enumerate(cut):
                    if c == TRANSPOSE_BEFORE:
                        transpose(b, parity, first)
                    if c == EXTRA_BEFORE:
                        pe.wait_ge(rest_lo_ready, b + 1)
                        if first:
                            pe.wait_ge(h_rest_lo_ready, 1)
                            pe.wait_ge(w_user_lo_ready, 1)
                        into = acc[parity][:, 0:UB]
                        nc.tensor.matmul(into, h_rest_split[:, :], rest_split[:, :], start=False, stop=False)
                        pe.wait_ge(norm_t_lo_ready, b + 1)
                        nc.tensor.matmul(into, w_user_hi[:, :], norm_t_hi[:, :], start=False, stop=False)
                        nc.tensor.matmul(into, w_user_lo[:, :], norm_t_hi[:, :], start=False, stop=False)
                        nc.tensor.matmul(into, w_user_hi[:, :], norm_t_lo[:, :], start=False, stop=False)
                    if c == 0 and not first and not second:
                        pe.wait_ge(relu_ready, b - 1)
                    k0 = sum(cut[:c])
                    if first:
                        pe.wait_ge(h_lo_ready, -(-(k0 + n) // HG))
                    pe.wait_ge(hi_ready, b * CHUNKS + (c + 1))
                    for t in range(n):
                        moving = adj_hi[:, c % HI_SLOTS, t * UB:(t + 1) * UB]
                        nc.tensor.matmul(acc[parity][:, 0:UB], h_hi[:, k0 + t, :], moving,
                                         start=(c == 0 and t == 0), stop=False)
                        nc.tensor.matmul(acc[parity][:, 0:UB], h_lo[:, k0 + t, :], moving, start=False, stop=False)
                    pe.wait_ge(lo_ready, b * CHUNKS + (c + 1))
                    for t in range(n):
                        end = c == len(cut) - 1 and t == n - 1
                        done = nc.tensor.matmul(acc[parity][:, 0:UB], h_hi[:, k0 + t, :],
                                                adj_lo[:, c % LO_SLOTS, t * UB:(t + 1) * UB], start=False, stop=end)
                    done.then_inc(chunk_used, 1)

            def transpose(b, parity, first):
                pe.wait_ge(x_in[parity], uses(b, parity))
                if first:
                    pe.wait_ge(identity_ready, 2)
                    pe.wait_ge(h_rest_ready, 1)
                else:
                    pe.wait_ge(result_ready, b)
                for t in range(XT):
                    done = nc.tensor.transpose(px[:, t * UT:(t + 1) * UT], x[0:UT, parity, t * HID:(t + 1) * HID],
                                               identity[0:UT, 0:UT])
                done.then_inc(x_transposed, 1)
                pe.wait_ge(norm_ready, b + 1)
                if not first:
                    pe.wait_ge(norm_t_lo_ready, b)
                for t in range(XT):
                    done = nc.tensor.transpose(pn[:, t * UT:(t + 1) * UT], norm[0:UT, t * HID:(t + 1) * HID],
                                               identity[0:UT, 0:UT])
                done.then_inc(norm_transposed, 1)

            pe.wait_ge(bias_lo_ready, 1)
            pe.wait_ge(weights_in, 16)
            for g in range(GROUPS):
                pe.wait_ge(feat_in[g % FEAT_SLOTS], 16 * (g // FEAT_SLOTS + 1))
                if g >= 2:
                    pe.wait_ge(h_lo_ready, g - 1)
                for i in range(2):
                    nc.tensor.matmul(ph[g % 2][:, i, 0:BANK_TILES * HID], ones[:, :], bias_split[:, :], start=True, stop=False)
                    for u in range(BANK_TILES):
                        t = i * BANK_TILES + u
                        done = nc.tensor.matmul(ph[g % 2][:, i, u * HID:(u + 1) * HID],
                                                feat[:, g % FEAT_SLOTS, t * P:(t + 1) * P], w_item[:, :],
                                                start=False, stop=u == BANK_TILES - 1)
                done.then_inc(h_product, 1)
            pe.wait_ge(later_weights_in, 16 * 3)
            nc.tensor.matmul(pn[0:REST, 0:HID], ones[:, 0:REST], bias_split[:, 0:HID], start=True, stop=False)
            nc.tensor.matmul(pn[0:REST, 0:HID], feat_rest[:, :], w_item[:, :], start=False, stop=True).then_inc(rest_product, 1)
            blocks(pe, one_block)


def kernel(x, adj, L0_gnn_item_feat, L0_gnn_W_item, L0_gnn_b_item, L0_gnn_W_user, L0_gnn_b_user):
    import numpy as np
    import concourse.bacc as bacc
    from concourse.bass_utils import run_bass_kernel_spmd

    x, adj = np.asarray(x), np.asarray(adj)
    cut = TILES * P
    x_tiles = np.zeros((BLOCKS, P, XT, HID), x.dtype)
    x_tiles[:, 0:UT] = x.reshape(BLOCKS, XT, UT, HID).transpose(0, 2, 1, 3)
    tiles = adj[:, 0:cut].reshape(BLOCKS, UB, TILES, P)
    adjt = np.zeros((BLOCKS, CHUNKS, P, ROW), adj.dtype)
    for c, n in enumerate(CUT):
        adjt[:, c, :, 0:n * UB].reshape(BLOCKS, P, n, UB)[...] = tiles[:, :, c * CT:c * CT + n].transpose(0, 3, 2, 1)
    arrays = {
        "adjt": adjt,
        "adjt_rest": np.ascontiguousarray(adj[:, cut:].reshape(BLOCKS, UB, REST).transpose(0, 2, 1)),
        "featt": np.ascontiguousarray(np.asarray(L0_gnn_item_feat).T),
        "xt": x_tiles.reshape(BLOCKS, P, XT * HID),
        "w_item_t": np.ascontiguousarray(np.asarray(L0_gnn_W_item).T),
        "w_user_t": np.ascontiguousarray(np.asarray(L0_gnn_W_user).T),
        "b_item": np.tile(np.asarray(L0_gnn_b_item), BANK_TILES).reshape(1, BANK_TILES * HID),
        "b_user": np.asarray(L0_gnn_b_user).reshape(HID, 1),
    }
    nc = bacc.Bacc("TRN2", target_bir_lowering=False, num_devices=1)
    args = [nc.dram_tensor(name, a.shape, mybir.dt.from_np(a.dtype), kind="ExternalInput").ap()
            for name, a in arrays.items()]
    out = nc.dram_tensor("out", (BLOCKS, HID, UB), mybir.dt.float32, kind="ExternalOutput").ap()
    gnn_kernel(nc, *args, out)
    r = run_bass_kernel_spmd(nc, [arrays], core_ids=[0])
    return np.ascontiguousarray(r.results[0]["out"].transpose(0, 2, 1)).reshape(USERS, HID)
```
